# Optimizing a Trainium2 kernel written in Bass

```python
import numpy as np
import jax
import jax.numpy as jnp

def _softmax(x, axis=-1):
    return jax.nn.softmax(x, axis=axis)

def _gelu(x):
    return jax.nn.gelu(x, approximate=True)

def _silu(x):
    return jax.nn.silu(x)

def _sigmoid(x):
    return jax.nn.sigmoid(x)

def _layernorm(x, axis=-1, eps=1e-05):
    m = jnp.mean(x, axis=axis, keepdims=True)
    v = jnp.var(x, axis=axis, keepdims=True)
    return (x - m) / jnp.sqrt(v + eps)

def _scatter_add(tgt, idx, src, axis=0):
    return tgt.at[idx].add(src)

def _segment_sum(src, seg, n):
    return jax.ops.segment_sum(src, seg, n)
kernel_name = 'mk_gnn_ffn_d1_gnn_r8_31bff4'

def setup_inputs(seed: int=0):
    np.random.seed(seed)
    _w = jnp.asarray

    def _rec_inputs():
        import jax
        import jax.numpy as jnp
        _gk = jax.random.key(seed)
        x = -0.0003713 + 1 * jax.random.normal(jax.random.fold_in(_gk, 1), (6250, 256), jnp.float32)
        src = jax.random.randint(jax.random.fold_in(_gk, 2), (100000,), 0, 6250, jnp.int32)
        dst = jax.random.randint(jax.random.fold_in(_gk, 3), (100000,), 0, 6250, jnp.int32)
        _o = jnp.argsort(dst, stable=True)
        src = src[_o]
        dst = dst[_o]
        edge_weight = jax.random.uniform(jax.random.fold_in(_gk, 12), (100000,), jnp.float32, 0.0, 1)
        return (x, src, dst, edge_weight)
    x, src, dst, edge_weight = _rec_inputs()

    def _L0_gnn_setup():
        import jax, jax.numpy as jnp
        import numpy as np
        N_NODES = 6250
        N_EDGES = 100000
        F_IN = 256
        F_OUT = 64
        HEADS = 4
        LEAKY_ALPHA = 0.2
        key = jax.random.key(seed)
        ks = jax.random.split(key, 8)
        x = jax.random.normal(ks[0], (N_NODES, F_IN), dtype=jnp.float32)
        W = jax.random.normal(ks[1], (HEADS, F_IN, F_OUT), dtype=jnp.float32) * 0.05
        a_self = jax.random.normal(ks[2], (HEADS, F_OUT), dtype=jnp.float32) * 0.05
        a_neigh = jax.random.normal(ks[3], (HEADS, F_OUT), dtype=jnp.float32) * 0.05
        bias = jnp.zeros((HEADS, F_OUT), dtype=jnp.float32)
        adj_val = jnp.ones((N_EDGES,), dtype=jnp.float32)
        edge_row = jax.random.randint(ks[4], (N_EDGES,), 0, N_NODES, dtype=jnp.int32)
        edge_col = jax.random.randint(ks[5], (N_EDGES,), 0, N_NODES, dtype=jnp.int32)
        return {'x': x, 'W': W, 'a_self': a_self, 'a_neigh': a_neigh, 'bias': bias, 'adj_val': adj_val, 'edge_row': edge_row, 'edge_col': edge_col}
    _L0_gnn_all = _L0_gnn_setup()
    _L0_gnn_in = {k: v for k, v in _L0_gnn_all.items() if k in ('W', 'a_self', 'a_neigh', 'bias')}
    del _L0_gnn_all

    def _L0_ffn_setup():
        import math
        import jax, jax.numpy as jnp
        import numpy as np
        CAPACITY_FACTOR = 1.25
        TOP_K = 2
        LN_EPS = 1e-05

        def _layer_norm(x, gamma, beta):
            mu = jnp.mean(x, axis=-1, keepdims=True)
            var = jnp.var(x, axis=-1, keepdims=True)
            return (x - mu) * jax.lax.rsqrt(var + LN_EPS) * gamma + beta
        key = jax.random.key(seed)
        ks = jax.random.split(key, 4)
        B, S, D, F, E = (8, 512, 256, 512, 8)
        x = jax.random.normal(ks[0], (B, S, D), dtype=jnp.float32)
        Wr = jax.random.normal(ks[1], (D, E), dtype=jnp.float32) / np.sqrt(D)
        br = jnp.zeros((E,), jnp.float32)
        W1 = jax.random.normal(ks[2], (E, D, F), dtype=jnp.float32) / np.sqrt(D)
        b1 = jnp.zeros((E, F), jnp.float32)
        W2 = jax.random.normal(ks[3], (E, F, D), dtype=jnp.float32) / np.sqrt(F)
        b2 = jnp.zeros((E, D), jnp.float32)
        gamma = jnp.ones((D,), jnp.float32)
        beta = jnp.zeros((D,), jnp.float32)
        return {'x': x, 'Wr': Wr, 'br': br, 'W1': W1, 'b1': b1, 'W2': W2, 'b2': b2, 'gamma': gamma, 'beta': beta}
    _L0_ffn_all = _L0_ffn_setup()
    _L0_ffn_in = {k: v for k, v in _L0_ffn_all.items() if k in ('Wr', 'br', 'W1', 'b1', 'W2', 'b2', 'gamma', 'beta')}
    del _L0_ffn_all
    return {'x': x, 'src': src, 'dst': dst, 'edge_weight': edge_weight, 'L0_gnn_W': _L0_gnn_in['W'], 'L0_gnn_a_self': _L0_gnn_in['a_self'], 'L0_gnn_a_neigh': _L0_gnn_in['a_neigh'], 'L0_gnn_bias': _L0_gnn_in['bias'], 'L0_ffn_Wr': _L0_ffn_in['Wr'], 'L0_ffn_br': _L0_ffn_in['br'], 'L0_ffn_W1': _L0_ffn_in['W1'], 'L0_ffn_b1': _L0_ffn_in['b1'], 'L0_ffn_W2': _L0_ffn_in['W2'], 'L0_ffn_b2': _L0_ffn_in['b2'], 'L0_ffn_gamma': _L0_ffn_in['gamma'], 'L0_ffn_beta': _L0_ffn_in['beta']}

def reference(x, src, dst, edge_weight, L0_gnn_W, L0_gnn_a_self, L0_gnn_a_neigh, L0_gnn_bias, L0_ffn_Wr, L0_ffn_br, L0_ffn_W1, L0_ffn_b1, L0_ffn_W2, L0_ffn_b2, L0_ffn_gamma, L0_ffn_beta):
    import jax
    import jax.numpy as jnp

    def _L0_gnn_ref(x, W, a_self, a_neigh, bias, adj_val, edge_row, edge_col):
        import jax, jax.numpy as jnp
        import numpy as np
        N_NODES = 6250
        N_EDGES = 100000
        F_IN = 256
        F_OUT = 64
        HEADS = 4
        LEAKY_ALPHA = 0.2
        N = x.shape[0]
        feats = jnp.einsum('nf,hfo->hno', x, W)
        s_self = jnp.einsum('hno,ho->hn', feats, a_self)
        s_neigh = jnp.einsum('hno,ho->hn', feats, a_neigh)
        z = s_self[:, edge_row] + s_neigh[:, edge_col]
        e = jnp.where(z > 0, z, LEAKY_ALPHA * z) * adj_val[None, :]

        def seg_softmax(e_h):
            m = jax.ops.segment_max(e_h, edge_row, num_segments=N)
            ex = jnp.exp(e_h - m[edge_row])
            s = jax.ops.segment_sum(ex, edge_row, num_segments=N)
            return ex / s[edge_row]
        alpha = jax.vmap(seg_softmax)(e)

        def aggregate(alpha_h, feat_h):
            return jax.ops.segment_sum(alpha_h[:, None] * feat_h[edge_col], edge_row, num_segments=N)
        out = jax.vmap(aggregate)(alpha, feats) + bias[:, None, :]
        out = jnp.transpose(out, (1, 0, 2)).reshape(N, -1)
        return jax.nn.relu(out)

    def _L0_ffn_ref(x, Wr, br, W1, b1, W2, b2, gamma, beta):
        import math
        import jax, jax.numpy as jnp
        import numpy as np
        CAPACITY_FACTOR = 1.25
        TOP_K = 2
        LN_EPS = 1e-05

        def _layer_norm(x, gamma, beta):
            mu = jnp.mean(x, axis=-1, keepdims=True)
            var = jnp.var(x, axis=-1, keepdims=True)
            return (x - mu) * jax.lax.rsqrt(var + LN_EPS) * gamma + beta
        B, S, D = x.shape
        E = Wr.shape[1]
        N = B * S
        K = TOP_K
        logits = jnp.mean(x, axis=1) @ Wr + br
        routing_weights = jax.nn.softmax(logits, axis=-1)
        capacity = float(math.ceil(N * CAPACITY_FACTOR / E))
        expected_loads = routing_weights.sum(axis=0) * (N / B)
        scale = jnp.where(expected_loads > capacity, capacity / expected_loads, 1.0)
        routing_weights = jax.nn.softmax(routing_weights * scale, axis=-1)
        rw_tok = jnp.broadcast_to(routing_weights[:, None, :], (B, S, E)).reshape(N, E)
        top_w, top_i = jax.lax.top_k(rw_tok, K)
        top_w = jax.nn.softmax(top_w, axis=-1)
        xf = x.reshape(N, D)
        h = jax.nn.gelu(jnp.einsum('nd,edf->enf', xf, W1) + b1[:, None, :], approximate=False)
        y = jnp.einsum('enf,efd->end', h, W2) + b2[:, None, :]
        w_dense = jnp.zeros((N, E), x.dtype).at[jnp.arange(N)[:, None], top_i].add(top_w)
        out = jnp.einsum('ne,end->nd', w_dense, y).reshape(B, S, D)
        out = _layer_norm(out + x, gamma, beta)
        return out
    x = x + _L0_gnn_ref(_layernorm(x, axis=-1), L0_gnn_W, L0_gnn_a_self, L0_gnn_a_neigh, L0_gnn_bias, edge_weight, src, dst)
    x = x + _L0_ffn_ref(_layernorm(x, axis=-1)[None], L0_ffn_Wr, L0_ffn_br, L0_ffn_W1, L0_ffn_b1, L0_ffn_W2, L0_ffn_b2, L0_ffn_gamma, L0_ffn_beta)[0]
    return x

_drawn_inputs = setup_inputs


def setup_inputs(seed=0):
    import zlib

    import numpy as np

    out = dict(_drawn_inputs(seed))
    spreads = {'L0_gnn_bias': (0.0, 0.1),
     'L0_ffn_br': (0.0, 0.1),
     'L0_ffn_b1': (0.0, 0.372),
     'L0_ffn_b2': (0.0, 0.1),
     'L0_ffn_gamma': (1.0, 0.2),
     'L0_ffn_beta': (0.0, 0.1)}
    factors = {'edge_weight': 3.907, 'L0_gnn_a_self': 4.987, 'L0_gnn_a_neigh': 3.012, 'L0_ffn_Wr': 8.0}
    for name, (base, spread) in spreads.items():
        noise = np.random.default_rng([zlib.crc32(name.encode()), seed]).standard_normal(out[name].shape)
        drawn = base * np.exp(spread * noise) if base else spread * noise
        out[name] = jnp.asarray(drawn.astype(out[name].dtype))
    for name, factor in factors.items():
        out[name] = (out[name] * factor).astype(out[name].dtype)
    return out
```

```python
from contextlib import ExitStack, contextmanager

import concourse.bass as bass
from concourse import mybir

F32 = mybir.dt.float32
BF16 = mybir.dt.bfloat16
I32 = mybir.dt.int32
U32 = mybir.dt.uint32
ALU = mybir.AluOpType
ACT = mybir.ActivationFunctionType
AX_X = mybir.AxisListType.X

P = 128
N_NODES, D = 6250, 256
N_EDGES = 100000
HEADS, F_OUT = 4, 64
LEAKY_ALPHA = 0.2
EXPERTS, FF = 8, 512
LN_EPS = 1e-05
CAPACITY = float(-(-N_NODES * 5 // (4 * EXPERTS)))
MASKED = -1e30
FLOOR = -5e29

TILES = -(-N_NODES // P)
PADDED = TILES * P
LAST = N_NODES - (TILES - 1) * P
ROWS = 32
BUCKETS = -(-N_NODES // ROWS)
DIGIT = 16
COLS = N_EDGES // P
TAIL = N_EDGES - COLS * P
COLS_PAD = 784
LOT = P // DIGIT
RANK_GROUP = 11
RANK_GROUPS = COLS // RANK_GROUP
GROUP = 4
GROUPS = 244
CHUNKS = GROUP * GROUPS
TABLE = HEADS * (F_OUT + 1) + HEADS
SN = HEADS * (F_OUT + 1)
assert COLS == RANK_GROUP * RANK_GROUPS and RANK_GROUPS % 2 == 1
assert (N_EDGES + BUCKETS * (P - 1)) // P <= CHUNKS
assert D == 2 * P and HEADS * ROWS == P and HEADS * F_OUT == D


class Link:

    def __init__(self, eng, sem):
        self.eng, self.sem, self.count, self.reg, self.per = eng, sem, 0, None, 0

    def at(self):
        return self.count if self.reg is None else self.reg * self.per + self.count

    def __call__(self, ins):
        ins.then_inc(self.sem, 1)
        self.count += 1
        self.eng.wait_ge(self.sem, self.at())

    @contextmanager
    def loop(self, reg, times, per):
        first = self.count
        self.reg, self.per = reg, per
        yield
        assert self.count - first == per, (self.count - first, per)
        self.reg, self.count = None, first + times * per


def gnn_ffn(nc, x, src, dst, edge_weight, W, a_self, a_neigh, bias, Wr, br, W1, b1, W2, b2, gamma, beta, out,
            table, self_scores, sorted_edges, bucket_list, gathered_nodes):
    with ExitStack() as ctx:
        def sb(name, shape, dt=F32):
            return ctx.enter_context(nc.sbuf_tensor(name, shape, dt))

        def sem(name):
            return ctx.enter_context(nc.semaphore(name))

        X = sb("X", [P, TILES, D])
        big = sb("big", [P, BUCKETS * (F_OUT + 1)])
        mid = sb("mid", [P, 16 * TABLE])
        low = sb("low", [P, 8192])
        slots = sb("slots", [P, CHUNKS, 4], I32)
        onehot_hi = big[:, 0:COLS_PAD * 8].bitcast(BF16).rearrange("p (c d) -> p c d", d=DIGIT)
        onehot_lo = big[:, COLS_PAD * 8:COLS_PAD * 16].bitcast(BF16).rearrange("p (c d) -> p c d", d=DIGIT)
        sums = big[:, :].rearrange("p (b f) -> p b f", f=F_OUT + 1)
        hnT = big[:, 0:2 * PADDED].rearrange("p (k n) -> p k n", k=2)
        row_i = mid[:, 0:COLS_PAD].bitcast(I32)
        col_i = mid[:, COLS_PAD:2 * COLS_PAD].bitcast(I32)
        wgt = mid[:, 2 * COLS_PAD:3 * COLS_PAD]
        digit_i = mid[:, 3 * COLS_PAD:4 * COLS_PAD].bitcast(I32)
        digit_f = mid[:, 4 * COLS_PAD:5 * COLS_PAD]
        onehot = mid[:, 0:RANK_GROUP * BUCKETS // 2].bitcast(BF16).rearrange("p (k b) -> p k b", b=BUCKETS)
        bucket_all = mid[:, 2048:3072].bitcast(I32)
        spread = mid[0:DIGIT, 3072:3584].rearrange("p (k b) -> p k b", k=2)
        hist = mid[:, 3584:3584 + P]
        rows_ring = mid[:, :].rearrange("p (s f) -> p s f", f=TABLE)
        w1 = mid[:, 0:2048].rearrange("p (e k f) -> p e k f", e=2, k=2)
        w2 = mid[:, 2048:4096].rearrange("p (e k d) -> p e k d", e=2, k=4)
        rec_f = low[:, 0:4 * COLS_PAD].rearrange("p (c w) -> p c w", w=4)
        rec_i = low[:, 0:4 * COLS_PAD].bitcast(I32).rearrange("p (c w) -> p c w", w=4)
        scores = low[:, 3136:3136 + 1024].rearrange("p (b n) -> p b n", b=2)
        probsT = low[:, 4160:4160 + 1024].rearrange("p (b n) -> p b n", b=2)
        probs = low[:, 5184:5184 + 1024].rearrange("p (b n) -> p b n", b=2)
        node_major = low[:, 0:2 * 14 * F_OUT].rearrange("p (b n f) -> p b n f", b=2, f=F_OUT)
        gnn_in = low[:, 2048:2048 + 2 * 7 * D].rearrange("p (b t d) -> p b t d", b=2, d=D)
        hidden = low[:, :].rearrange("p (b f n) -> p b f n", b=2, f=8)
        w_in = low[:, 6208:6208 + 2 * D].rearrange("p (k d) -> p k d", k=2)
        a_all = low[:, 6720:6720 + 2 * D].rearrange("p (k d) -> p k d", k=2)
        mask = low[:, 7232:7488].rearrange("p (b n) -> p b n", b=2)
        in_bucketT = low[:, 7488:7744].rearrange("p (b n) -> p b n", b=2)
        slots_f = slots[:, :, :].bitcast(F32)
        fin = slots_f.rearrange("p c w -> p (c w)")[:, 0:4 * D].rearrange("p (t d) -> p t d", d=D)

        pid_i = sb("pid_i", [P, 1], I32)
        pid_d = sb("pid_d", [P, 2], I32)
        pid_f = sb("pid_f", [P, 2])
        col_id = sb("col_id", [P, 256], I32)
        col_hi = sb("col_hi", [P, P], I32)
        col_hf = sb("col_hf", [P, P])
        iota_f = sb("iota_f", [P, 256])
        iota_b = sb("iota_b", [P, 256], BF16)
        chunk_i = sb("chunk_i", [P, 8], I32)
        chunk_f = sb("chunk_f", [P, 8])
        ident = sb("ident", [P, P])
        ident_b = sb("ident_b", [P, P], BF16)
        before = sb("before", [P, P])
        before_b = sb("before_b", [P, P], BF16)
        rest_b = sb("rest_b", [P, P], BF16)
        ones = sb("ones", [P, 256])
        same_lot = sb("same_lot", [P, P])
        same_digit = sb("same_digit", [P, DIGIT])
        eps = sb("eps", [P, 1])

        bucket_f = sb("bucket_f", [P, COLS_PAD])
        cnt = sb("cnt", [DIGIT, 6, DIGIT])
        cnt_i = sb("cnt_i", [DIGIT, 2, DIGIT], I32)
        base = sb("base", [P, BUCKETS])
        scratch = sb("scratch", [P, BUCKETS])
        bucket_of = sb("bucket_of", [P, 8])
        bucket_of_i = sb("bucket_of_i", [P, 8], I32)
        pos = sb("pos", [P, RANK_GROUP])
        pos_i = sb("pos_i", [P, 3, RANK_GROUP], I32)
        staged = sb("staged", [P, 2, RANK_GROUP * 4], I32)
        bucket_row = sb("bucket_row", [1, 1024], I32)
        reset = sb("reset", [P, CHUNKS])

        w_prod = sb("w_prod", [P, D])
        w_ext = sb("w_ext", [P, 2, D + 2 * HEADS])
        stats = sb("stats", [P, TILES, 6])
        moments = sb("moments", [P, 6, TILES])
        xn = sb("xn", [P, 2, D])
        xnT = sb("xnT", [P, 2, D])
        table_rows = sb("table_rows", [P, 2, TABLE])
        ss_nodes = sb("ss_nodes", [P, TILES, HEADS])
        ss_rows = sb("ss_rows", [P, BUCKETS, HEADS])

        idx = sb("idx", [P, 16], I32)
        in_bucket = sb("in_bucket", [P, 2, P], BF16)
        ss_blocks = sb("ss_blocks", [P, 2, 16])
        ez = sb("ez", [P, 2, 3, 16])
        mx = sb("mx", [P, 2, 24])
        shrink = sb("shrink", [P, 2, GROUP])

        rden = sb("rden", [P, BUCKETS])
        bias_all = sb("bias_all", [P, F_OUT])
        mean_col = sb("mean_col", [P, 2])
        mean_all = sb("mean_all", [P, 2, P])
        wr = sb("wr", [P, 2, EXPERTS])
        rt = sb("rt", [P, 16, EXPERTS])
        top_i = sb("top_i", [P, EXPERTS], U32)
        b1_col = sb("b1_col", [P, 2, 4])
        b2_all = sb("b2_all", [P, 2, D])
        gb_all = sb("gb_all", [P, 2, D])
        fin_m = sb("fin_m", [P, 4, 6])
        fin_v = sb("fin_v", [P, 6, 4])

        bank = [ctx.enter_context(nc.psum_tensor(f"bank{i}", [P, 512], F32)) for i in range(7)]
        bank_b = ctx.enter_context(nc.psum_tensor("bank_b", [P, 512], F32))
        turned_b = bank_b[:, 0:64].bitcast(BF16)
        ss_edges = bank[6][:, 0:16]

        x_loaded = sem("x_loaded")
        edges_loaded = sem("edges_loaded")
        tail_loaded = sem("tail_loaded")
        weights_loaded = sem("weights_loaded")
        slots_cleared = sem("slots_cleared")
        scattered = [sem("scattered_a"), sem("scattered_b")]
        slots_loaded = sem("slots_loaded")
        buckets_stored = sem("buckets_stored")
        buckets_loaded = sem("buckets_loaded")
        table_stored = [sem("table_stored_a"), sem("table_stored_b")]
        ss_stored = sem("ss_stored")
        ss_loaded = sem("ss_loaded")
        rows_gathered = [sem(f"rows_gathered_{j}") for j in range(4)]
        nodes_stored = [sem("nodes_stored_a"), sem("nodes_stored_b")]
        nodes_loaded = [sem("nodes_loaded_a"), sem("nodes_loaded_b")]
        experts_loaded = sem("experts_loaded")
        out_stored = sem("out_stored")
        vec_step = sem("vec_step")
        act_step = sem("act_step")
        pool_step = sem("pool_step")
        rows_cleared = sem("rows_cleared")
        nodes_cleared = sem("nodes_cleared")
        iota_ready = sem("iota_ready")
        pool_cleared = sem("pool_cleared")
        consts_ready = sem("consts_ready")
        digits_ready = sem("digits_ready")
        hist_ready = sem("hist_ready")
        hist_masked = sem("hist_masked")
        hist_folded = sem("hist_folded")
        totals_ready = sem("totals_ready")
        prefix_ready = sem("prefix_ready")
        spread_ready = sem("spread_ready")
        base_ready = sem("base_ready")
        base_copied = sem("base_copied")
        onehot_built = sem("onehot_built")
        ranks_summed = sem("ranks_summed")
        ranks_read = sem("ranks_read")
        buckets_known = sem("buckets_known")
        ranks_ready = sem("ranks_ready")
        records_staged = sem("records_staged")
        w_ext_ready = sem("w_ext_ready")
        var_ready = sem("var_ready")
        std_ready = sem("std_ready")
        stats_done = sem("stats_done")
        xn_ready = sem("xn_ready")
        xn_turned = sem("xn_turned")
        xnT_ready = sem("xnT_ready")
        feats_ready = sem("feats_ready")
        table_built = sem("table_built")
        edge_start = sem("edge_start")
        indices_staged = sem("indices_staged")
        mask_built = sem("mask_built")
        in_bucket_built = sem("in_bucket_built")
        in_bucket_turned = sem("in_bucket_turned")
        in_bucketT_copied = sem("in_bucketT_copied")
        ss_summed = sem("ss_summed")
        scores_built = sem("scores_built")
        scores_turned = sem("scores_turned")
        max_ready = sem("max_ready")
        probsT_ready = sem("probsT_ready")
        shrink_ready = sem("shrink_ready")
        probs_turned = sem("probs_turned")
        probs_copied = sem("probs_copied")
        parts_ready = sem("parts_ready")
        parts_added = sem("parts_added")
        nodes_built = sem("nodes_built")
        nodes_added = sem("nodes_added")
        mean_ready = sem("mean_ready")
        mean_spread = sem("mean_spread")
        logits_ready = sem("logits_ready")
        exp_in = sem("exp_in")
        exp_out = sem("exp_out")
        route_known = sem("route_known")
        w2_scaled = sem("w2_scaled")
        hidden_summed = sem("hidden_summed")
        hidden_ready = sem("hidden_ready")
        moe_ready = sem("moe_ready")
        moe_read = sem("moe_read")
        out_built = sem("out_built")

        block = ctx.enter_context(nc.Block())

        @block.sync
        def _(sp):
            head = COLS * P
            for dram, tile in ((src, row_i), (dst, col_i), (edge_weight, wgt)):
                sp.dma_start(tile[:, 0:COLS], dram[0:head].rearrange("(p c) -> p c", p=P)).then_inc(edges_loaded, 16)
            sp.wait_ge(rows_cleared, 1)
            for dram, tile in ((src, row_i), (dst, col_i), (edge_weight, wgt)):
                sp.dma_start(tile[0:TAIL, COLS:COLS + 1],
                             dram[head:N_EDGES].rearrange("(p c) -> p c", c=1)).then_inc(tail_loaded, 16)
            sp.wait_ge(nodes_cleared, 1)
            full = (TILES - 1) * P
            sp.dma_start(X[:, 0:TILES - 1, :], x[0:full, :].rearrange("(t p) d -> p t d", p=P)).then_inc(x_loaded, 16)
            sp.dma_start(X[0:LAST, TILES - 1, :], x[full:N_NODES, :]).then_inc(x_loaded, 16)
            for k in range(2):
                sp.dma_start(w_in[:, k, :].rearrange("p (h o) -> p h o", h=HEADS),
                             W[:, k * P:(k + 1) * P, :].rearrange("h f o -> f h o")).then_inc(weights_loaded, 16)
            for k, a in enumerate((a_self, a_neigh)):
                sp.dma_start(a_all[:, k, :], a.rearrange("h o -> (h o)").partition_broadcast(P)).then_inc(weights_loaded, 16)
            for h in range(HEADS):
                sp.dma_start(bias_all[h * ROWS:(h + 1) * ROWS, :],
                             bias[h, :].partition_broadcast(ROWS)).then_inc(weights_loaded, 16)
            sp.dma_start(wr[:, :, :], Wr.rearrange("(k p) e -> p k e", p=P)).then_inc(weights_loaded, 16)
            sp.dma_start(rt[:, 0, :], br.partition_broadcast(P)).then_inc(weights_loaded, 16)
            sp.dma_start(gb_all[:, 0, :], gamma.partition_broadcast(P)).then_inc(weights_loaded, 16)
            sp.dma_start(gb_all[:, 1, :], beta.partition_broadcast(P)).then_inc(weights_loaded, 16)
            sp.wait_ge(buckets_known, 1)
            sp.dma_start(bucket_list.rearrange("(p j) -> p j", p=P), bucket_of_i[:, :]).then_inc(buckets_stored, 16)
            sp.wait_ge(buckets_stored, 16)
            sp.dma_start(bucket_row[:, :], bucket_list.rearrange("(a c) -> a c", a=1)).then_inc(buckets_loaded, 16)
            sp.dma_start(bucket_all[:, :], bucket_list.partition_broadcast(P)).then_inc(buckets_loaded, 16)
            with sp.Fori(0, (TILES - 1) // 2) as i:
                for b in range(2):
                    sp.wait_ge(table_built, 2 * i + b + 1)
                    sp.dma_start(table[bass.ds(i * (2 * P) + b * P, P), :], table_rows[:, b, :]).then_inc(table_stored[b], 16)
            sp.wait_ge(table_built, TILES)
            sp.dma_start(table[(TILES - 1) * P:PADDED, :], table_rows[:, 0, :]).then_inc(table_stored[0], 16)
            sp.dma_start(self_scores.rearrange("(t p) h -> p t h", p=P), ss_nodes[:, :, :]).then_inc(ss_stored, 16)
            sp.wait_ge(ss_stored, 16)
            for c in range(GROUP):
                sp.dma_start(ss_rows[c * ROWS:(c + 1) * ROWS, :, :],
                             self_scores.rearrange("(b r) h -> r b h", r=ROWS)).then_inc(ss_loaded, 16)
            sp.wait_ge(scattered[0], 16 * (RANK_GROUP * (RANK_GROUPS + 1) // 2 + 1))
            sp.wait_ge(scattered[1], 16 * (RANK_GROUP * (RANK_GROUPS - 1) // 2))
            sp.dma_start(slots[:, :, :], sorted_edges.rearrange("(p c) w -> p c w", p=P)).then_inc(slots_loaded, 16)
            for g in range(14):
                b = g % 2
                sp.wait_ge(nodes_built, g + 1)
                for h in range(HEADS):
                    sp.dma_start(
                        gathered_nodes[g * 14 * ROWS:(g + 1) * 14 * ROWS, h * F_OUT:(h + 1) * F_OUT]
                        .rearrange("(n r) f -> r n f", r=ROWS),
                        node_major[h * ROWS:(h + 1) * ROWS, b, :, :]).then_inc(nodes_stored[b], 16)
            sp.wait_ge(nodes_stored[0], 16 * HEADS * 7)
            sp.wait_ge(nodes_stored[1], 16 * HEADS * 7)
            for g in range(7):
                b = g % 2
                if g >= 2:
                    sp.wait_ge(nodes_added, g - 1)
                sp.dma_start(gnn_in[:, b, :, :],
                             gathered_nodes[g * 7 * P:(g + 1) * 7 * P, :].rearrange("(t p) d -> p t d", p=P)
                             ).then_inc(nodes_loaded[b], 16)
            sp.wait_ge(route_known, 1)
            for e in range(2):
                k = sp.value_load(top_i[0:1, e:e + 1].bitcast(I32), min_val=0, max_val=EXPERTS - 1)
                sp.dma_start(w1[:, e, :, :], W1[bass.ds(k, 1), :, :].rearrange("a (k p) f -> p (a k) f", p=P)
                             ).then_inc(experts_loaded, 16)
                sp.dma_start(w2[:, e, :, :], W2[bass.ds(k, 1), :, :].rearrange("a (k p) d -> p (a k) d", p=P)
                             ).then_inc(experts_loaded, 16)
                sp.dma_start(b1_col[:, e, :], b1[bass.ds(k, 1), :].rearrange("a (k p) -> p (a k)", p=P),
                             allow_slow_non_contiguous=True).then_inc(experts_loaded, 16)
                sp.dma_start(b2_all[:, e, :], b2[bass.ds(k, 1), :].rearrange("a d -> (a d)").partition_broadcast(P)
                             ).then_inc(experts_loaded, 16)
            with sp.Fori(0, 12) as i:
                sp.wait_ge(out_built, i + 1)
                sp.dma_start(out[bass.ds(i * 512, 512), :].rearrange("(t p) d -> p t d", p=P),
                             fin[:, :, :]).then_inc(out_stored, 16)
            sp.wait_ge(out_built, 13)
            sp.dma_start(out[(TILES - 1) * P:N_NODES, :], fin[0:LAST, 0, :]).then_inc(out_stored, 16)
            sp.wait_ge(out_stored, 16 * 13)

        @block.gpsimd
        def _(pool):
            step = Link(pool, pool_step)
            pool.memset(row_i[:, COLS:COLS_PAD], -1).then_inc(rows_cleared, 1)
            pool.iota(pid_i[:, :], pattern=[[0, 1]], base=0, channel_multiplier=1).then_inc(iota_ready, 1)
            pool.iota(col_id[:, :], pattern=[[1, 256]], base=0, channel_multiplier=0).then_inc(iota_ready, 1)
            pool.iota(chunk_i[:, :], pattern=[[1, 8]], base=0, channel_multiplier=8).then_inc(iota_ready, 1)
            step(pool.memset(ident[:, :], 1.0))
            pool.affine_select(out=ident[:, :], in_=ident[:, :], compare_op=ALU.is_equal, fill=0.0, base=0,
                               pattern=[[-1, P]], channel_multiplier=1).then_inc(iota_ready, 1)
            step(pool.memset(before[:, :], 1.0))
            pool.affine_select(out=before[:, :], in_=before[:, :], compare_op=ALU.is_gt, fill=0.0, base=0,
                               pattern=[[1, P]], channel_multiplier=-1).then_inc(iota_ready, 1)
            step(pool.memset(slots[:, :, :], 0))
            step(pool.memset(slots_f[:, :, 0], -1.0))
            pool.dma_start(sorted_edges.rearrange("(p c) w -> p c w", p=P), slots[:, :, :]).then_inc(slots_cleared, 16)
            pool.memset(table_rows[:, :, :], 1.0).then_inc(pool_cleared, 1)
            pool.memset(ss_blocks[:, :, :], 0.0).then_inc(pool_cleared, 1)
            pool.wait_ge(slots_cleared, 16)

            def scatter(g, b, n=RANK_GROUP):
                step(pool.tensor_copy(staged[:, b, 0:4 * n].rearrange("p (c w) -> p c w", w=4),
                                      rec_i[:, bass.ds(g * RANK_GROUP, n) if not isinstance(g, int)
                                            else slice(g * RANK_GROUP, g * RANK_GROUP + n), :]))
                pool.sem_inc(records_staged, 1)
                for k in range(n):
                    rows = P if n == RANK_GROUP else TAIL
                    pool.indirect_dma_start(
                        sorted_edges, bass.IndirectOffsetOnAxis(ap=staged[0:rows, b, 4 * k + 3:4 * k + 4], axis=0),
                        staged[0:rows, b, 4 * k:4 * k + 4], None).then_inc(scattered[b], 16)

            for g in range(2):
                pool.wait_ge(ranks_ready, g + 1)
                scatter(g, g)
            with pool.Fori(1, RANK_GROUPS // 2) as i, step.loop(i - 1, RANK_GROUPS // 2 - 1, 2):
                for b in range(2):
                    pool.wait_ge(ranks_ready, 2 * i + b + 1)
                    pool.wait_ge(scattered[b], i * (16 * RANK_GROUP))
                    scatter(2 * i + b, b)
            half = RANK_GROUPS // 2
            pool.wait_ge(ranks_ready, RANK_GROUPS)
            pool.wait_ge(scattered[0], half * 16 * RANK_GROUP)
            scatter(RANK_GROUPS - 1, 0)
            pool.wait_ge(ranks_ready, RANK_GROUPS + 1)
            pool.wait_ge(scattered[0], (half + 1) * 16 * RANK_GROUP)
            scatter(RANK_GROUPS, 0, 1)

            pool.memset(big[:, :], 0.0).then_inc(pool_cleared, 1)
            pool.wait_ge(slots_loaded, 16)
            pool.wait_ge(edge_start, 2)
            pool.wait_ge(table_stored[0], 16 * (TILES + 1) // 2)
            pool.wait_ge(table_stored[1], 16 * (TILES // 2))

            def gather(g, j):
                at = slice(g * GROUP, (g + 1) * GROUP) if isinstance(g, int) else bass.ds(g * GROUP, GROUP)
                step(pool.tensor_copy(idx[:, GROUP * j:GROUP * (j + 1)], slots[:, at, 1]))
                pool.sem_inc(indices_staged, 1)
                for c in range(GROUP * j, GROUP * (j + 1)):
                    pool.indirect_dma_start(rows_ring[:, c, :], None, table,
                                            bass.IndirectOffsetOnAxis(ap=idx[:, c:c + 1], axis=0)
                                            ).then_inc(rows_gathered[j], 16)

            for j in range(4):
                gather(j, j)
            with pool.Fori(1, GROUPS // 4) as i, step.loop(i - 1, GROUPS // 4 - 1, 4):
                for j in range(4):
                    pool.wait_ge(parts_ready, 4 * i + (j - 3))
                    pool.wait_ge(rows_gathered[j], i * (16 * GROUP))
                    gather(4 * i + j, j)

        @block.tensor
        def _(pe):
            pe.wait_ge(digits_ready, 1)
            lot_hist = bank[0][:, 0:P]
            hi_lots = big[:, 0:COLS_PAD * 8].bitcast(BF16)
            lo_lots = big[:, COLS_PAD * 8:COLS_PAD * 16].bitcast(BF16)
            for k in range(7):
                pe.matmul(lot_hist, hi_lots[:, k * P:(k + 1) * P], lo_lots[:, k * P:(k + 1) * P],
                          start=(k == 0), stop=False, skip_group_check=True)
            with pe.Fori(1, COLS_PAD // LOT // 7) as i:
                for k in range(7):
                    mm = pe.matmul(lot_hist, hi_lots[:, bass.ds(i * (7 * P) + k * P, P)],
                                   lo_lots[:, bass.ds(i * (7 * P) + k * P, P)], start=False, stop=False,
                                   skip_group_check=True)
                mm.then_inc(hist_ready, 1)
            pe.wait_ge(hist_masked, 1)
            pe.matmul(bank[1][0:DIGIT, 0:P], same_digit[:, :], hist[:, :], start=True, stop=True).then_inc(hist_folded, 1)
            pe.wait_ge(totals_ready, 1)
            pe.matmul(bank[1][0:DIGIT, 128:129], before[0:DIGIT, 0:DIGIT], cnt[:, 3, DIGIT - 1:DIGIT],
                      start=True, stop=True).then_inc(prefix_ready, 1)
            pe.wait_ge(spread_ready, 1)
            pe.matmul(bank[1][:, 256:256 + BUCKETS], ones[0:DIGIT, 0:P], spread[:, 0, 0:BUCKETS],
                      start=True, stop=True).then_inc(base_ready, 1)
            running = bank[2][:, 0:BUCKETS]
            pe.matmul(running, ones[0:DIGIT, 0:P], spread[:, 1, 0:BUCKETS], start=True, stop=False, skip_group_check=True)

            def rank(n, k):
                pe.wait_ge(onehot_built, n + 1)
                pe.matmul(running, before_b[:, :], onehot[:, k, :], start=False, stop=False,
                          skip_group_check=True).then_inc(ranks_summed, 1)
                pe.wait_ge(ranks_read, n + 1)
                pe.matmul(running, rest_b[:, :], onehot[:, k, :], start=False, stop=False, skip_group_check=True)

            with pe.Fori(0, RANK_GROUPS) as i:
                for k in range(RANK_GROUP):
                    rank(i * RANK_GROUP + k, k)
            rank(COLS, 0)

            def turn(n, b):
                pe.wait_ge(xn_ready, n + 1)
                for k in range(2):
                    mm = pe.transpose(bank[b][:, k * P:(k + 1) * P], xn[:, b, k * P:(k + 1) * P], ident[:, :])
                mm.then_inc(xn_turned, 1)

            def project(n, b):
                pe.wait_ge(xnT_ready, n + 1)
                if not isinstance(n, int) or n >= 2:
                    pe.wait_ge(table_built, n - 1)
                for k in range(2):
                    mm = pe.matmul(bank[3 + b][:, 0:D + 2 * HEADS], xnT[:, b, k * P:(k + 1) * P], w_ext[:, k, :],
                                   start=(k == 0), stop=(k == 1))
                mm.then_inc(feats_ready, 1)

            pe.wait_ge(w_ext_ready, 1)
            turn(0, 0)
            for n in range(2):
                turn(n + 1, 1 - n)
                project(n, n)
            with pe.Fori(1, (TILES - 1) // 2) as i:
                for b in range(2):
                    turn(2 * i + b + 1, 1 - b)
                    project(2 * i + b, b)
            project(TILES - 1, 0)

            def turn_in_bucket(g, b):
                pe.wait_ge(in_bucket_built, g + 1)
                if not isinstance(g, int) or g >= 1:
                    pe.wait_ge(in_bucketT_copied, g)
                pe.transpose(turned_b, in_bucket[:, b, :], ident_b[:, :]).then_inc(in_bucket_turned, 1)

            def sum_ss(g, b):
                pe.wait_ge(in_bucketT_copied, g + 1)
                if not isinstance(g, int) or g >= 1:
                    pe.wait_ge(scores_built, g)
                pe.matmul(ss_edges, in_bucketT[:, b, :], ss_blocks[:, b, :], start=True, stop=True
                          ).then_inc(ss_summed, 1)

            def turn_scores(g, b):
                pe.wait_ge(scores_built, g + 1)
                if not isinstance(g, int) or g >= 2:
                    pe.wait_ge(probsT_ready, g - 1)
                for c in range(GROUP):
                    mm = pe.transpose(bank[b][:, c * P:(c + 1) * P], scores[:, b, c * P:(c + 1) * P], ident[:, :])
                mm.then_inc(scores_turned, 1)

            def turn_probs(g, b):
                pe.wait_ge(probsT_ready, g + 1)
                if not isinstance(g, int) or g >= 2:
                    pe.wait_ge(probs_copied, g - 1)
                for c in range(GROUP):
                    mm = pe.transpose(bank[2 + b][:, c * P:(c + 1) * P], probsT[:, b, c * P:(c + 1) * P], ident[:, :])
                mm.then_inc(probs_turned, 1)

            def sum_parts(g, j, b):
                pe.wait_ge(probs_copied, g + 1)
                if not isinstance(g, int) or g >= 2:
                    pe.wait_ge(parts_added, (g - 1) * GROUP)
                for c in range(GROUP):
                    for h in range(HEADS):
                        mm = pe.matmul(bank[4 + b][h * ROWS:(h + 1) * ROWS, c * (F_OUT + 1):(c + 1) * (F_OUT + 1)],
                                       probs[:, b, c * P + h * ROWS:c * P + (h + 1) * ROWS],
                                       rows_ring[:, GROUP * j + c, h * (F_OUT + 1):(h + 1) * (F_OUT + 1)],
                                       start=True, stop=True, tile_position=(0, h * ROWS))
                mm.then_inc(parts_ready, 1)

            def edge_step(g, j, first=False, last=False):
                b = j % 2
                if not first:
                    turn_probs(g - 1, 1 - b)
                if not last:
                    turn_in_bucket(g + 1, 1 - b)
                turn_scores(g, b)
                if not last:
                    sum_ss(g + 1, 1 - b)
                if not first:
                    sum_parts(g - 1, (j - 1) % 4, 1 - b)

            turn_in_bucket(0, 0)
            sum_ss(0, 0)
            for g in range(4):
                edge_step(g, g, first=(g == 0))
            with pe.Fori(1, GROUPS // 4 - 1) as i:
                for j in range(4):
                    edge_step(4 * i + j, j)
            for g in range(GROUPS - 4, GROUPS):
                edge_step(g, g % 4, last=(g == GROUPS - 1))
            turn_probs(GROUPS - 1, 1)
            sum_parts(GROUPS - 1, 3, 1)

            mean_sum = bank[6][:, 0:2]

            def turn_tokens(n, b, rows, first=False):
                pe.wait_ge(xn_ready, n + (TILES + 1))
                if not first:
                    pe.wait_ge(xnT_ready, n + (TILES - 1))
                for k in range(2):
                    pe.matmul(mean_sum[:, k:k + 1], xn[0:rows, b, k * P:(k + 1) * P], ones[0:rows, 0:1],
                              start=first, stop=False, skip_group_check=True)
                for k in range(2):
                    mm = pe.transpose(bank[b][:, k * P:(k + 1) * P], xn[:, b, k * P:(k + 1) * P], ident[:, :])
                mm.then_inc(xn_turned, 1)

            turn_tokens(0, 0, LAST, first=True)
            with pe.Fori(0, (TILES - 1) // 2) as i:
                for b in range(2):
                    turn_tokens(2 * i + b + 1, 1 - b, P)
            pe.wait_ge(mean_spread, 1)
            for k in range(2):
                mm = pe.matmul(bank[6][:, 8:8 + EXPERTS], mean_all[:, k, :], wr[:, k, :], start=(k == 0), stop=(k == 1))
            mm.then_inc(logits_ready, 1)

            def hidden_layer(s, b, n):
                for f in range(8):
                    q = s * 8 + f
                    if not isinstance(s, int) or q >= 4:
                        pe.wait_ge(hidden_ready, q - 3)
                    at = slice(s * 512, s * 512 + n) if isinstance(s, int) else bass.ds(s * 512, n)
                    for k in range(2):
                        mm = pe.matmul(bank[f % 4][:, 0:n], w1[:, f // 4, k, (f % 4) * P:(f % 4 + 1) * P],
                                       hnT[:, k, at], start=(k == 0), stop=(k == 1))
                    mm.then_inc(hidden_summed, 1)

            def output_layer(s, b, tiles):
                pe.wait_ge(hidden_ready, 8 * s + 8)
                for t in range(tiles):
                    if not isinstance(s, int) or 4 * s + t >= 2:
                        pe.wait_ge(moe_read, s * 4 + (t - 1))
                    for f in range(8):
                        mm = pe.matmul(bank[4 + t % 2][:, 0:D], hidden[:, b, f, t * P:(t + 1) * P],
                                       w2[:, f // 4, f % 4, :], start=(f == 0), stop=(f == 7))
                    mm.then_inc(moe_ready, 1)

            pe.wait_ge(experts_loaded, 16 * 8)
            pe.wait_ge(xnT_ready, 2 * TILES)
            hidden_layer(0, 0, 512)
            pe.wait_ge(w2_scaled, 1)
            hidden_layer(1, 1, 512)
            output_layer(0, 0, 4)
            with pe.Fori(1, 6) as i:
                for b in range(2):
                    hidden_layer(2 * i + b, b, 512)
                    output_layer(2 * i + b - 1, 1 - b, 4)
            hidden_layer(12, 0, P)
            output_layer(11, 1, 4)
            output_layer(12, 0, 1)

        @block.scalar
        def _(act):
            act.wait_ge(var_ready, 1)
            act.activation(moments[:, 4, :], moments[:, 3, :], ACT.Sqrt, bias=eps[:, 0:1]).then_inc(std_ready, 1)

            def copy_xnT(n, b):
                act.wait_ge(xn_turned, n + 1)
                if not isinstance(n, int) or n >= 2:
                    act.wait_ge(feats_ready, n - 1)
                act.copy(xnT[:, b, :], bank[b][:, 0:D]).then_inc(xnT_ready, 1)

            copy_xnT(0, 0)
            copy_xnT(1, 1)
            with act.Fori(1, (TILES - 1) // 2) as i:
                for b in range(2):
                    copy_xnT(2 * i + b, b)
            copy_xnT(TILES - 1, 0)

            act.wait_ge(pool_cleared, 2)
            act.wait_ge(ss_loaded, 16 * GROUP)
            act.wait_ge(buckets_loaded, 32)

            def copy_in_bucket(g, b):
                if not isinstance(g, int) or g >= 2:
                    act.wait_ge(ss_summed, g - 1)
                for c in range(GROUP):
                    k = act.value_load(bucket_row[0:1, g * GROUP + c:g * GROUP + c + 1] if isinstance(g, int)
                                       else bucket_row[0:1, bass.ds(g * GROUP + c, 1)], min_val=0, max_val=BUCKETS - 1)
                    act.copy(ss_blocks[c * ROWS:(c + 1) * ROWS, b, c * HEADS:(c + 1) * HEADS].unsqueeze(1),
                             ss_rows[c * ROWS:(c + 1) * ROWS, bass.ds(k, 1), :])
                act.wait_ge(in_bucket_turned, g + 1)
                act.copy(in_bucketT[:, b, :], turned_b).then_inc(in_bucketT_copied, 1)

            def copy_probs(g, b):
                act.wait_ge(probs_turned, g + 1)
                if not isinstance(g, int) or g >= 2:
                    act.wait_ge(parts_ready, g - 1)
                act.copy(probs[:, b, :], bank[2 + b][:, :]).then_inc(probs_copied, 1)

            def exponentials(g, b):
                act.wait_ge(max_ready, g + 1)
                if not isinstance(g, int) or g >= 2:
                    act.wait_ge(probs_turned, g - 1)
                for c in range(GROUP):
                    e = act.activation(probsT[:, b, c * P:(c + 1) * P], bank[b][:, c * P:(c + 1) * P], ACT.Exp,
                                       bias=mx[:, b, 16 + c:17 + c])
                e.then_inc(probsT_ready, 1)
                if not isinstance(g, int) or g >= 2:
                    act.wait_ge(parts_added, (g - 1) * GROUP)
                act.activation(shrink[:, b, :], mx[:, b, 20:24], ACT.Exp).then_inc(shrink_ready, 1)

            def edge_step(g, j, first=False, last=False):
                b = j % 2
                if not first:
                    copy_probs(g - 1, 1 - b)
                if not last:
                    copy_in_bucket(g + 1, 1 - b)
                exponentials(g, b)

            copy_in_bucket(0, 0)
            for g in range(4):
                edge_step(g, g, first=(g == 0))
            with act.Fori(1, GROUPS // 4 - 1) as i:
                for j in range(4):
                    edge_step(4 * i + j, j)
            for g in range(GROUPS - 4, GROUPS):
                edge_step(g, g % 4, last=(g == GROUPS - 1))
            copy_probs(GROUPS - 1, 1)

            act.wait_ge(var_ready, 2)
            act.activation(moments[:, 4, :], moments[:, 3, :], ACT.Sqrt, bias=eps[:, 0:1]).then_inc(std_ready, 1)

            def copy_hnT(n, b, at):
                act.wait_ge(xn_turned, n + (TILES + 1))
                act.copy(hnT[:, :, at], bank[b][:, 0:D].rearrange("p (k n) -> p k n", k=2)).then_inc(xnT_ready, 1)

            copy_hnT(0, 0, slice((TILES - 1) * P, PADDED))
            with act.Fori(0, (TILES - 1) // 2) as i:
                for b in range(2):
                    copy_hnT(2 * i + b + 1, 1 - b, bass.ds(i * (2 * P) + b * P, P))
            for k in range(3):
                act.wait_ge(exp_in, k + 1)
                n = 2 if k == 2 else EXPERTS
                act.activation(rt[:, 2 + k, 0:n], rt[:, 5 + k, 0:n], ACT.Exp).then_inc(exp_out, 1)

            act.wait_ge(experts_loaded, 16 * 8)

            def hidden_layer(s, b, n):
                for f in range(8):
                    act.wait_ge(hidden_summed, s * 8 + f + 1)
                    if not isinstance(s, int) or s >= 2:
                        if f == 0:
                            act.wait_ge(moe_ready, (s - 1) * 4)
                    act.activation(hidden[:, b, f, 0:n], bank[f % 4][:, 0:n], ACT.Gelu,
                                   bias=b1_col[:, f // 4, f % 4:f % 4 + 1]).then_inc(hidden_ready, 1)

            def deviations(s):
                act.wait_ge(var_ready, s + 3)
                act.activation(fin_v[:, 4, :], fin_v[:, 3, :], ACT.Sqrt, bias=eps[:, 0:1]).then_inc(std_ready, 1)

            hidden_layer(0, 0, 512)
            hidden_layer(1, 1, 512)
            deviations(0)
            with act.Fori(1, 6) as i:
                for b in range(2):
                    hidden_layer(2 * i + b, b, 512)
                    deviations(2 * i + b - 1)
            hidden_layer(12, 0, P)
            deviations(11)
            deviations(12)

        @block.vector
        def _(vec):
            step = Link(vec, vec_step)
            vec.memset(X[96:P, TILES - 1, :], 0.0).then_inc(nodes_cleared, 1)
            vec.memset(ones[:, :], 1.0).then_inc(consts_ready, 1)
            vec.memset(eps[:, :], LN_EPS).then_inc(consts_ready, 1)
            vec.wait_ge(iota_ready, 5)
            vec.tensor_copy(iota_f[:, :], col_id[:, :]).then_inc(consts_ready, 1)
            vec.tensor_copy(iota_b[:, :], col_id[:, :]).then_inc(consts_ready, 1)
            vec.tensor_copy(chunk_f[:, :], chunk_i[:, :]).then_inc(consts_ready, 1)
            vec.tensor_copy(ident_b[:, :], ident[:, :]).then_inc(consts_ready, 1)
            vec.tensor_copy(before_b[:, :], before[:, :]).then_inc(consts_ready, 1)
            vec.tensor_scalar(rest_b[:, :], before[:, :], -1.0, 1.0, ALU.mult, ALU.add).then_inc(consts_ready, 1)
            vec.tensor_scalar(pid_d[:, 0:1], pid_i[:, :], 4, None, ALU.arith_shift_right).then_inc(consts_ready, 1)
            vec.tensor_scalar(pid_d[:, 1:2], pid_i[:, :], DIGIT - 1, None, ALU.bitwise_and).then_inc(consts_ready, 1)
            vec.tensor_scalar(col_hi[:, :], col_id[:, 0:P], 4, None, ALU.arith_shift_right).then_inc(consts_ready, 1)
            vec.wait_ge(consts_ready, 11)
            step(vec.tensor_copy(pid_f[:, :], pid_d[:, :]))
            step(vec.tensor_copy(col_hf[:, :], col_hi[:, :]))
            vec.tensor_scalar(same_lot[:, :], col_hf[:, :], pid_f[:, 0:1], None, ALU.is_equal).then_inc(consts_ready, 1)
            vec.tensor_scalar(same_digit[:, :], iota_f[:, 0:DIGIT], pid_f[:, 1:2], None,
                              ALU.is_equal).then_inc(consts_ready, 1)
            vec.wait_ge(consts_ready, 13)

            vec.wait_ge(edges_loaded, 48)
            vec.wait_ge(tail_loaded, 48)
            iota_16 = iota_f[:, 0:DIGIT].unsqueeze(1).broadcast_to([P, COLS_PAD, DIGIT])

            def one_hots(dest):
                step(vec.tensor_copy(digit_f, digit_i))
                return vec.tensor_tensor(dest, digit_f.unsqueeze(2).broadcast_to([P, COLS_PAD, DIGIT]), iota_16,
                                         ALU.is_equal)

            step(vec.tensor_scalar(digit_i, row_i, 9, None, ALU.arith_shift_right))
            step(one_hots(onehot_hi))
            step(vec.tensor_scalar(digit_i, row_i, 5, DIGIT - 1, ALU.arith_shift_right, ALU.bitwise_and))
            one_hots(onehot_lo).then_inc(digits_ready, 1)
            vec.wait_ge(digits_ready, 1)
            step(vec.tensor_scalar(digit_i, row_i, 5, None, ALU.arith_shift_right))
            step(vec.tensor_copy(bucket_f[:, :], digit_i))
            step(vec.tensor_scalar(digit_i, row_i, ROWS - 1, None, ALU.bitwise_and))
            step(vec.memset(rec_i[:, COLS:COLS_PAD, :], 0))
            step(vec.tensor_copy(rec_f[:, :, 0], digit_i))
            step(vec.tensor_copy(rec_i[:, 0:COLS, 1], col_i[:, 0:COLS]))
            step(vec.tensor_copy(rec_f[:, 0:COLS, 2], wgt[:, 0:COLS]))
            step(vec.tensor_copy(rec_i[0:TAIL, COLS:COLS + 1, 1], col_i[0:TAIL, COLS:COLS + 1]))
            step(vec.tensor_copy(rec_f[0:TAIL, COLS:COLS + 1, 2], wgt[0:TAIL, COLS:COLS + 1]))

            vec.wait_ge(hist_ready, COLS_PAD // LOT // 7 - 1)
            vec.tensor_tensor(hist[:, :], bank[0][:, 0:P], same_lot[:, :], ALU.mult).then_inc(hist_masked, 1)
            vec.wait_ge(hist_folded, 1)
            step(vec.tensor_reduce(cnt[:, 0, :], bank[1][0:DIGIT, 0:P].rearrange("h (c l) -> h l c", l=DIGIT), AX_X, ALU.add))
            step(vec.tensor_scalar(cnt[:, 1, :], cnt[:, 0, :], float(P - 1), None, ALU.add))
            step(vec.tensor_copy(cnt_i[:, 0, :], cnt[:, 1, :]))
            step(vec.tensor_scalar(cnt_i[:, 1, :], cnt_i[:, 0, :], 7, None, ALU.arith_shift_right))
            step(vec.tensor_copy(cnt[:, 2, :], cnt_i[:, 1, :]))
            vec.tensor_tensor_scan(cnt[:, 3, :], ones[0:DIGIT, 0:DIGIT], cnt[:, 2, :], 0.0, ALU.mult,
                                   ALU.add).then_inc(totals_ready, 1)
            vec.wait_ge(prefix_ready, 1)
            vec.wait_ge(totals_ready, 1)
            step(vec.tensor_tensor(cnt[:, 4, :], cnt[:, 3, :], cnt[:, 2, :], ALU.subtract))
            step(vec.tensor_copy(cnt[:, 5, 0:1], bank[1][0:DIGIT, 128:129]))
            step(vec.tensor_scalar(cnt[:, 4, :], cnt[:, 4, :], cnt[:, 5, 0:1], None, ALU.add))
            step(vec.tensor_tensor(spread[:, 0, :].rearrange("k (h l) -> k h l", l=DIGIT),
                                   cnt[:, 4, :].unsqueeze(1).broadcast_to([DIGIT, DIGIT, DIGIT]),
                                   ident[0:DIGIT, 0:DIGIT].unsqueeze(2).broadcast_to([DIGIT, DIGIT, DIGIT]), ALU.mult))
            vec.tensor_scalar(spread[:, 1, :], spread[:, 0, :], float(P), None, ALU.mult).then_inc(spread_ready, 1)
            vec.wait_ge(base_ready, 1)
            step(vec.tensor_copy(base[:, :], bank[1][:, 256:256 + BUCKETS]))

            def build_onehot(n, k):
                at = slice(n, n + 1) if isinstance(n, int) else bass.ds(n, 1)
                vec.tensor_scalar(onehot[:, k, :], iota_b[:, 0:BUCKETS], bucket_f[:, at], None,
                                  ALU.is_equal).then_inc(onehot_built, 1)

            def read_rank(n, k):
                at = slice(n, n + 1) if isinstance(n, int) else bass.ds(n, 1)
                vec.wait_ge(ranks_summed, n + 1)
                vec.scalar_tensor_tensor(scratch[:, :], iota_b[:, 0:BUCKETS], bucket_f[:, at], bank[2][:, 0:BUCKETS],
                                         ALU.is_equal, ALU.mult, accum_out=pos[:, k:k + 1]).then_inc(ranks_read, 1)

            def place(first, n):
                step(vec.tensor_copy(pos_i[:, 0, 0:n], pos[:, 0:n]))
                step(vec.tensor_scalar(pos_i[:, 1, 0:n], pos_i[:, 0, 0:n], P - 1, None, ALU.bitwise_and))
                step(vec.tensor_scalar(pos_i[:, 2, 0:n], pos_i[:, 0, 0:n], 7, None, ALU.arith_shift_right))
                at = slice(first, first + n) if isinstance(first, int) else bass.ds(first, n)
                vec.scalar_tensor_tensor(rec_i[:, at, 3], pos_i[:, 1, 0:n], float(CHUNKS), pos_i[:, 2, 0:n],
                                         ALU.mult, ALU.add).then_inc(ranks_ready, 1)

            build_onehot(0, 0)
            with vec.Fori(0, RANK_GROUPS) as i, step.loop(i, RANK_GROUPS, 3):
                for k in range(RANK_GROUP):
                    build_onehot(i * RANK_GROUP + (k + 1), (k + 1) % RANK_GROUP)
                    if k:
                        vec.wait_ge(ranks_read, i * RANK_GROUP + k)
                    read_rank(i * RANK_GROUP + k, k)
                vec.wait_ge(ranks_read, (i + 1) * RANK_GROUP)
                place(i * RANK_GROUP, RANK_GROUP)
            read_rank(COLS, 0)
            vec.wait_ge(ranks_read, COLS + 1)
            place(COLS, 1)

            for j in range(8):
                step(vec.scalar_tensor_tensor(scratch[:, :], base[:, :], chunk_f[:, j:j + 1], ones[:, 0:BUCKETS],
                                              ALU.is_le, ALU.mult, accum_out=bucket_of[:, j:j + 1]))
            vec.tensor_scalar(bucket_of_i[:, :], bucket_of[:, :], -1.0, None, ALU.add).then_inc(buckets_known, 1)

            vec.wait_ge(weights_loaded, 16 * 12)
            for k in range(2):
                step(vec.tensor_copy(w_ext[:, k, 0:D], w_in[:, k, :]))
                for at, a in ((D, 1), (D + HEADS, 0)):
                    step(vec.tensor_tensor(w_prod[:, :], w_in[:, k, :], a_all[:, a, :], ALU.mult))
                    step(vec.tensor_reduce(w_ext[:, k, at:at + HEADS], w_prod[:, :].rearrange("p (h o) -> p h o", h=HEADS),
                                           AX_X, ALU.add))
            vec.memset(scratch[:, 0:1], 0.0).then_inc(w_ext_ready, 1)

            def layer_norm_terms(stats, m, which):
                even, odd = stats[:, :, 0:3], stats[:, :, 3:6]
                step(vec.tensor_tensor(m[:, 0, :], even[:, :, 1], odd[:, :, 1], ALU.add))
                step(vec.tensor_tensor(m[:, 1, :], even[:, :, 1], odd[:, :, 1], ALU.subtract))
                step(vec.tensor_tensor(m[:, 2, :], even[:, :, 2], odd[:, :, 2], ALU.add))
                step(vec.tensor_tensor(m[:, 1, :], m[:, 1, :], m[:, 1, :], ALU.mult))
                step(vec.tensor_scalar(m[:, 1, :], m[:, 1, :], 0.25, None, ALU.mult))
                vec.scalar_tensor_tensor(m[:, 3, :], m[:, 2, :], 1.0 / D, m[:, 1, :], ALU.mult,
                                         ALU.add).then_inc(var_ready, 1)
                vec.wait_ge(std_ready, which)
                step(vec.reciprocal(m[:, 4, :], m[:, 4, :]))
                step(vec.scalar_tensor_tensor(m[:, 5, :], m[:, 0, :], -0.5, m[:, 4, :], ALU.mult, ALU.mult))

            vec.wait_ge(x_loaded, 32)
            with vec.Fori(0, 7) as i:
                for t in range(7):
                    at = bass.ds(i * 7 + t, 1)
                    last = vec.bn_stats(stats[:, at, :].rearrange("p a s -> p (a s)"),
                                        X[:, at, :].rearrange("p a d -> p (a d)"))
                last.then_inc(stats_done, 1)
            vec.wait_ge(stats_done, 7)
            layer_norm_terms(stats, moments, 1)

            def normalize(t, b):
                at = slice(t, t + 1) if isinstance(t, int) else bass.ds(t, 1)
                vec.tensor_scalar(xn[:, b:b + 1, :], X[:, at, :], moments[:, 4, at], moments[:, 5, at],
                                  ALU.mult, ALU.add).then_inc(xn_ready, 1)

            def build_table(n, b):
                vec.wait_ge(feats_ready, n + 1)
                vec.tensor_copy(table_rows[:, b, 0:SN].rearrange("p (h f) -> p h f", h=HEADS)[:, :, 0:F_OUT],
                                bank[3 + b][:, 0:D].rearrange("p (h f) -> p h f", h=HEADS))
                at = slice(n, n + 1) if isinstance(n, int) else bass.ds(n, 1)
                vec.tensor_copy(ss_nodes[:, at, :], bank[3 + b][:, D + HEADS:D + 2 * HEADS].unsqueeze(1))
                vec.tensor_copy(table_rows[:, b, SN:TABLE], bank[3 + b][:, D:D + HEADS]).then_inc(table_built, 1)

            vec.wait_ge(pool_cleared, 1)
            normalize(0, 0)
            normalize(1, 1)
            build_table(0, 0)
            vec.wait_ge(xn_turned, 1)
            normalize(2, 0)
            build_table(1, 1)
            with vec.Fori(1, (TILES - 1) // 2) as i:
                for b in range(2):
                    vec.wait_ge(xn_turned, 2 * i + b)
                    normalize(2 * i + b + 1, 1 - b)
                    vec.wait_ge(table_stored[b], i * 16)
                    build_table(2 * i + b, b)
            vec.wait_ge(table_stored[0], 16 * (TILES // 2))
            build_table(TILES - 1, 0)

            vec.wait_ge(buckets_loaded, 32)
            step(vec.tensor_tensor(reset[:, 1:CHUNKS], bucket_all[:, 1:CHUNKS], bucket_all[:, 0:CHUNKS - 1],
                                   ALU.not_equal))
            step(vec.tensor_scalar(reset[:, 1:CHUNKS], reset[:, 1:CHUNKS], MASKED, None, ALU.mult))
            vec.memset(reset[:, 0:1], MASKED).then_inc(edge_start, 1)
            vec.memset(mx[:, 1, 8:9], MASKED).then_inc(edge_start, 1)
            vec.wait_ge(edge_start, 2)
            vec.wait_ge(slots_loaded, 16)
            vec.wait_ge(pool_cleared, 3)
            iota_rows = iota_f[:, 0:ROWS].unsqueeze(1).broadcast_to([P, GROUP, ROWS])

            def chunks(g):
                return slice(g * GROUP, (g + 1) * GROUP) if isinstance(g, int) else bass.ds(g * GROUP, GROUP)

            def build_in_bucket(g, b):
                if not isinstance(g, int) or g >= 2:
                    vec.wait_ge(in_bucket_turned, g - 1)
                vec.tensor_tensor(in_bucket[:, b, :].rearrange("p (c r) -> p c r", r=ROWS),
                                  slots_f[:, chunks(g), 0:1].broadcast_to([P, GROUP, ROWS]), iota_rows,
                                  ALU.is_equal).then_inc(in_bucket_built, 1)
                vec.wait_ge(in_bucket_built, g + 1)
                vec.tensor_scalar(mask[:, b, :], in_bucket[:, b, :], -MASKED, MASKED, ALU.mult,
                                  ALU.add).then_inc(mask_built, 1)

            def build_scores(g, j, turn):
                b = j % 2
                vec.wait_ge(ss_summed, g + 1)
                vec.wait_ge(rows_gathered[j], (turn + 1) * (16 * GROUP))
                z, lrelu, e = (ez[:, b, k, :].rearrange("p (c h) -> p c h", h=HEADS) for k in range(3))
                step(vec.tensor_tensor(z, ss_edges.rearrange("p (c h) -> p c h", h=HEADS),
                                       rows_ring[:, GROUP * j:GROUP * (j + 1), SN:TABLE], ALU.add))
                step(vec.scalar_tensor_tensor(lrelu, z, LEAKY_ALPHA, z, ALU.mult, ALU.max))
                step(vec.tensor_tensor(e, lrelu, slots_f[:, chunks(g), 2:3].broadcast_to([P, GROUP, HEADS]), ALU.mult))
                if not isinstance(g, int) or g >= 2:
                    vec.wait_ge(scores_turned, g - 1)
                vec.wait_ge(mask_built, g + 1)
                shape = [P, GROUP, HEADS, ROWS]
                vec.tensor_tensor(scores[:, b, :].rearrange("p (c h r) -> p c h r", c=GROUP, h=HEADS),
                                  mask[:, b, :].rearrange("p (c r) -> p c r", r=ROWS).unsqueeze(2).broadcast_to(shape),
                                  e.unsqueeze(3).broadcast_to(shape), ALU.add).then_inc(scores_built, 1)

            def build_max(g, b):
                vec.wait_ge(scores_turned, g + 1)
                if not isinstance(g, int) or g >= 2:
                    vec.wait_ge(shrink_ready, g - 1)
                m, last = mx[:, b, :], mx[:, 1 - b, 8:9]
                step(vec.tensor_reduce(m[:, 0:4], bank[b][:, :].rearrange("p (c e) -> p c e", c=GROUP), AX_X, ALU.max))
                step(vec.tensor_scalar(m[:, 0:4], m[:, 0:4], FLOOR, None, ALU.max))
                step(vec.tensor_tensor_scan(m[:, 5:9], reset[:, chunks(g)], m[:, 0:4], last, ALU.add, ALU.max))
                step(vec.tensor_copy(m[:, 4:5], last))
                step(vec.tensor_tensor(m[:, 12:16], reset[:, chunks(g)], m[:, 4:8], ALU.add))
                step(vec.tensor_tensor(m[:, 20:24], m[:, 12:16], m[:, 5:9], ALU.subtract))
                vec.tensor_scalar(m[:, 16:20], m[:, 5:9], -1.0, None, ALU.mult).then_inc(max_ready, 1)

            def add_part(g, b, c):
                at = slice(g * GROUP + c, g * GROUP + c + 1) if isinstance(g, int) else bass.ds(g * GROUP + c, 1)
                k = vec.value_load(bucket_row[0:1, at], min_val=0, max_val=BUCKETS - 1)
                if c == 0:
                    vec.wait_ge(parts_ready, g + 1)
                    vec.wait_ge(shrink_ready, g + 1)
                if not isinstance(g, int) or g or c:
                    vec.wait_ge(parts_added, g * GROUP + c)
                here = sums[:, bass.ds(k, 1), :]
                vec.scalar_tensor_tensor(here, here, shrink[:, b, c:c + 1],
                                         bank[4 + b][:, c * (F_OUT + 1):(c + 1) * (F_OUT + 1)].unsqueeze(1),
                                         ALU.mult, ALU.add).then_inc(parts_added, 1)

            def edge_step(g, j, turn, first=False, ahead=True):
                b = j % 2
                build_scores(g, j, turn)
                if ahead:
                    build_in_bucket(g + 2, b)
                build_max(g, b)
                if not first:
                    for c in range(GROUP):
                        add_part(g - 1, 1 - b, c)

            build_in_bucket(0, 0)
            build_in_bucket(1, 1)
            for g in range(4):
                edge_step(g, g, 0, first=(g == 0))
            with vec.Fori(1, GROUPS // 4 - 1) as i, step.loop(i - 1, GROUPS // 4 - 2, 4 * 9):
                for j in range(4):
                    edge_step(4 * i + j, j, i)
            for g in range(GROUPS - 4, GROUPS):
                edge_step(g, g % 4, g // 4, ahead=(g < GROUPS - 2))
            for c in range(GROUP):
                add_part(GROUPS - 1, 1, c)
            vec.wait_ge(parts_added, CHUNKS)

            step(vec.tensor_scalar(rden[:, :], sums[:, :, F_OUT], 1e-30, None, ALU.max))
            step(vec.reciprocal(rden[:, :], rden[:, :]))
            for g in range(14):
                b = g % 2
                if g >= 2:
                    vec.wait_ge(nodes_stored[b], 16 * HEADS * (g // 2))
                at, shape = slice(14 * g, 14 * g + 14), [P, 14, F_OUT]
                nm = node_major[:, b, :, :]
                step(vec.tensor_tensor(nm, sums[:, at, 0:F_OUT], rden[:, at].unsqueeze(2).broadcast_to(shape), ALU.mult))
                step(vec.tensor_tensor(nm, nm, bias_all[:, :].unsqueeze(1).broadcast_to(shape), ALU.add))
                vec.tensor_scalar(nm, nm, 0.0, None, ALU.max).then_inc(nodes_built, 1)
            for g in range(7):
                b = g % 2
                vec.wait_ge(nodes_loaded[b], 16 * (g // 2 + 1))
                at = slice(7 * g, 7 * g + 7)
                vec.tensor_tensor(X[:, at, :], X[:, at, :], gnn_in[:, b, :, :], ALU.add).then_inc(nodes_added, 1)
                vec.wait_ge(nodes_added, g + 1)
                for t in range(7 * g, 7 * g + 7):
                    last = vec.bn_stats(stats[:, t, :], X[:, t, :])
                last.then_inc(stats_done, 1)
            vec.wait_ge(stats_done, 14)
            layer_norm_terms(stats, moments, 2)
            normalize(TILES - 1, 0)
            with vec.Fori(0, (TILES - 1) // 2) as i:
                for b in range(2):
                    vec.wait_ge(xn_turned, 2 * i + (TILES + b))
                    normalize(2 * i + b, 1 - b)

            vec.wait_ge(xn_turned, 2 * TILES)
            step(vec.tensor_scalar(mean_col[:, :], bank[6][:, 0:2], 1.0 / N_NODES, None, ALU.mult))
            vec.tensor_copy(mean_all[:, :, :], mean_col[:, :].unsqueeze(2).broadcast_to([P, 2, P])).then_inc(mean_spread, 1)
            vec.wait_ge(logits_ready, 1)

            def softmax(k, values, n, result):
                step(vec.tensor_reduce(rt[:, 8, 0:1], values, AX_X, ALU.max))
                vec.tensor_scalar(rt[:, 5 + k, 0:n], values, rt[:, 8, 0:1], None, ALU.subtract).then_inc(exp_in, 1)
                vec.wait_ge(exp_out, k + 1)
                step(vec.tensor_reduce(rt[:, 8, 1:2], rt[:, 2 + k, 0:n], AX_X, ALU.add))
                step(vec.reciprocal(rt[:, 8, 2:3], rt[:, 8, 1:2]))
                step(vec.tensor_scalar(result, rt[:, 2 + k, 0:n], rt[:, 8, 2:3], None, ALU.mult))

            step(vec.tensor_tensor(rt[:, 1, :], bank[6][:, 8:8 + EXPERTS], rt[:, 0, :], ALU.add))
            softmax(0, rt[:, 1, :], EXPERTS, rt[:, 9, :])
            step(vec.tensor_scalar(rt[:, 10, :], rt[:, 9, :], float(N_NODES), CAPACITY, ALU.mult, ALU.max))
            step(vec.reciprocal(rt[:, 11, :], rt[:, 10, :]))
            step(vec.scalar_tensor_tensor(rt[:, 12, :], rt[:, 11, :], CAPACITY, rt[:, 9, :], ALU.mult, ALU.mult))
            softmax(1, rt[:, 12, :], EXPERTS, rt[:, 13, :])
            step(vec.max(rt[:, 14, :], rt[:, 13, :]))
            vec.max_index(top_i[:, :], rt[:, 14, :], rt[:, 13, :]).then_inc(route_known, 1)
            softmax(2, rt[:, 14, 0:2], 2, rt[:, 15, 0:2])
            vec.wait_ge(experts_loaded, 16 * 8)
            for e in range(2):
                step(vec.tensor_scalar(w2[:, e, :, :], w2[:, e, :, :], rt[:, 15, e:e + 1], None, ALU.mult))
            step(vec.tensor_scalar(b2_all[:, 0, :], b2_all[:, 0, :], rt[:, 15, 0:1], None, ALU.mult))
            vec.scalar_tensor_tensor(b2_all[:, 0, :], b2_all[:, 1, :], rt[:, 15, 1:2], b2_all[:, 0, :], ALU.mult,
                                     ALU.add).then_inc(w2_scaled, 1)
            vec.wait_ge(w2_scaled, 1)

            def finish(s, tiles):
                if not isinstance(s, int) or s >= 1:
                    vec.wait_ge(out_stored, s * 16)
                for t in range(tiles):
                    q = s * 4 + t
                    at = slice(q, q + 1) if isinstance(q, int) else bass.ds(q, 1)
                    f = fin[:, t:t + 1, :]
                    step(vec.tensor_scalar(f, X[:, at, :], moments[:, 4, at], moments[:, 5, at], ALU.mult, ALU.add))
                    vec.wait_ge(moe_ready, q + 1)
                    vec.tensor_tensor(f, f, bank[4 + t % 2][:, 0:D].unsqueeze(1), ALU.add).then_inc(moe_read, 1)
                    vec.wait_ge(moe_read, q + 1)
                    step(vec.tensor_tensor(f, f, b2_all[:, 0:1, :], ALU.add))
                    step(vec.bn_stats(fin_m[:, t, :], fin[:, t, :]))
                layer_norm_terms(fin_m, fin_v, s + 3)
                for t in range(tiles):
                    step(vec.tensor_scalar(fin[:, t, :], fin[:, t, :], fin_v[:, 4, t:t + 1], fin_v[:, 5, t:t + 1],
                                           ALU.mult, ALU.add))
                f, shape = fin[:, 0:tiles, :], [P, tiles, D]
                at = slice(s * 4, s * 4 + tiles) if isinstance(s, int) else bass.ds(s * 4, tiles)
                step(vec.tensor_tensor(f, f, gb_all[:, 0:1, :].broadcast_to(shape), ALU.mult))
                step(vec.tensor_tensor(f, f, gb_all[:, 1:2, :].broadcast_to(shape), ALU.add))
                vec.tensor_tensor(f, f, X[:, at, :], ALU.add).then_inc(out_built, 1)

            step(vec.memset(fin_m[:, :, :], 0.0))
            finish(0, 4)
            with vec.Fori(1, 12) as i, step.loop(i - 1, 11, 4 * 3 + 7 + 4 + 2):
                finish(i, 4)
            finish(12, 1)


_INS = ["x", "src", "dst", "edge_weight", "L0_gnn_W", "L0_gnn_a_self", "L0_gnn_a_neigh", "L0_gnn_bias", "L0_ffn_Wr",
        "L0_ffn_br", "L0_ffn_W1", "L0_ffn_b1", "L0_ffn_W2", "L0_ffn_b2", "L0_ffn_gamma", "L0_ffn_beta"]


def kernel(**inputs):
    import numpy as _np
    import concourse.bacc as _bacc
    from concourse import mybir as _mybir
    from concourse.bass_utils import run_bass_kernel_spmd as _run

    nc = _bacc.Bacc("TRN2", target_bir_lowering=False, num_devices=1)
    arrays, args = {}, []
    for name in _INS:
        a = _np.ascontiguousarray(inputs[name])
        arrays[f"in_{name}_dram"] = a
        args.append(nc.dram_tensor(f"in_{name}_dram", a.shape, _mybir.dt.from_np(a.dtype), kind="ExternalInput").ap())
    args.append(nc.dram_tensor("out_0_dram", (N_NODES, D), F32, kind="ExternalOutput").ap())
    for name, shape, dt in (("table", (PADDED, TABLE), F32), ("self_scores", (PADDED, HEADS), F32),
                            ("sorted_edges", (P * CHUNKS, 4), I32), ("bucket_list", (1024,), I32),
                            ("gathered_nodes", (PADDED, D), F32)):
        args.append(nc.dram_tensor(name, shape, dt).ap())
    gnn_ffn(nc, *args)
    r = _run(nc, [arrays], core_ids=[0])
    return r.results[0]["out_0_dram"]
```
